# Optimizing a Trainium2 kernel written in Bass

```python
import numpy as np
import jax
import jax.numpy as jnp

def _softmax(x, axis=-1):
    return jax.nn.softmax(x, axis=axis)

def _gelu(x):
    return jax.nn.gelu(x, approximate=True)

def _silu(x):
    return jax.nn.silu(x)

def _sigmoid(x):
    return jax.nn.sigmoid(x)

def _layernorm(x, axis=-1, eps=1e-05):
    m = jnp.mean(x, axis=axis, keepdims=True)
    v = jnp.var(x, axis=axis, keepdims=True)
    return (x - m) / jnp.sqrt(v + eps)

def _scatter_add(tgt, idx, src, axis=0):
    return tgt.at[idx].add(src)

def _segment_sum(src, seg, n):
    return jax.ops.segment_sum(src, seg, n)
kernel_name = 'mk_dlrm_tower_d1_rec_r8_44c2a1'

def setup_inputs(seed: int=0):
    np.random.seed(seed)
    _w = jnp.asarray

    def _rec_inputs():
        import jax
        import jax.numpy as jnp
        _tk = jax.random.key(seed)
        dense_ctx = jax.random.normal(jax.random.fold_in(_tk, 190), (512, 16), jnp.float32)
        ids = jnp.stack([jax.random.randint(jax.random.fold_in(_tk, 200 + f), (512,), 0, v, jnp.int32) for f, v in enumerate([1000, 125000, 1000, 1000, 1000, 1250, 1000, 1000, 1000, 1250, 12500, 1250, 1000, 12500, 1250, 1250, 1250, 12500, 1250, 1000, 12500, 1000, 12500, 1000, 12500, 1000, 12500, 1000, 1000, 1000, 12500, 1000])], axis=1)
        tbl_0 = 0.05 * jax.random.normal(jax.random.fold_in(_tk, 500 + 0), (1000, 128), jnp.float32)
        tbl_1 = 0.05 * jax.random.normal(jax.random.fold_in(_tk, 500 + 1), (125000, 128), jnp.float32)
        tbl_2 = 0.05 * jax.random.normal(jax.random.fold_in(_tk, 500 + 2), (1000, 128), jnp.float32)
        tbl_3 = 0.05 * jax.random.normal(jax.random.fold_in(_tk, 500 + 3), (1000, 128), jnp.float32)
        tbl_4 = 0.05 * jax.random.normal(jax.random.fold_in(_tk, 500 + 4), (1000, 128), jnp.float32)
        tbl_5 = 0.05 * jax.random.normal(jax.random.fold_in(_tk, 500 + 5), (1250, 128), jnp.float32)
        tbl_6 = 0.05 * jax.random.normal(jax.random.fold_in(_tk, 500 + 6), (1000, 128), jnp.float32)
        tbl_7 = 0.05 * jax.random.normal(jax.random.fold_in(_tk, 500 + 7), (1000, 128), jnp.float32)
        tbl_8 = 0.05 * jax.random.normal(jax.random.fold_in(_tk, 500 + 8), (1000, 128), jnp.float32)
        tbl_9 = 0.05 * jax.random.normal(jax.random.fold_in(_tk, 500 + 9), (1250, 128), jnp.float32)
        tbl_10 = 0.05 * jax.random.normal(jax.random.fold_in(_tk, 500 + 10), (12500, 128), jnp.float32)
        tbl_11 = 0.05 * jax.random.normal(jax.random.fold_in(_tk, 500 + 11), (1250, 128), jnp.float32)
        tbl_12 = 0.05 * jax.random.normal(jax.random.fold_in(_tk, 500 + 12), (1000, 128), jnp.float32)
        tbl_13 = 0.05 * jax.random.normal(jax.random.fold_in(_tk, 500 + 13), (12500, 128), jnp.float32)
        tbl_14 = 0.05 * jax.random.normal(jax.random.fold_in(_tk, 500 + 14), (1250, 128), jnp.float32)
        tbl_15 = 0.05 * jax.random.normal(jax.random.fold_in(_tk, 500 + 15), (1250, 128), jnp.float32)
        tbl_16 = 0.05 * jax.random.normal(jax.random.fold_in(_tk, 500 + 16), (1250, 128), jnp.float32)
        tbl_17 = 0.05 * jax.random.normal(jax.random.fold_in(_tk, 500 + 17), (12500, 128), jnp.float32)
        tbl_18 = 0.05 * jax.random.normal(jax.random.fold_in(_tk, 500 + 18), (1250, 128), jnp.float32)
        tbl_19 = 0.05 * jax.random.normal(jax.random.fold_in(_tk, 500 + 19), (1000, 128), jnp.float32)
        tbl_20 = 0.05 * jax.random.normal(jax.random.fold_in(_tk, 500 + 20), (12500, 128), jnp.float32)
        tbl_21 = 0.05 * jax.random.normal(jax.random.fold_in(_tk, 500 + 21), (1000, 128), jnp.float32)
        tbl_22 = 0.05 * jax.random.normal(jax.random.fold_in(_tk, 500 + 22), (12500, 128), jnp.float32)
        tbl_23 = 0.05 * jax.random.normal(jax.random.fold_in(_tk, 500 + 23), (1000, 128), jnp.float32)
        tbl_24 = 0.05 * jax.random.normal(jax.random.fold_in(_tk, 500 + 24), (12500, 128), jnp.float32)
        tbl_25 = 0.05 * jax.random.normal(jax.random.fold_in(_tk, 500 + 25), (1000, 128), jnp.float32)
        tbl_26 = 0.05 * jax.random.normal(jax.random.fold_in(_tk, 500 + 26), (12500, 128), jnp.float32)
        tbl_27 = 0.05 * jax.random.normal(jax.random.fold_in(_tk, 500 + 27), (1000, 128), jnp.float32)
        tbl_28 = 0.05 * jax.random.normal(jax.random.fold_in(_tk, 500 + 28), (1000, 128), jnp.float32)
        tbl_29 = 0.05 * jax.random.normal(jax.random.fold_in(_tk, 500 + 29), (1000, 128), jnp.float32)
        tbl_30 = 0.05 * jax.random.normal(jax.random.fold_in(_tk, 500 + 30), (12500, 128), jnp.float32)
        tbl_31 = 0.05 * jax.random.normal(jax.random.fold_in(_tk, 500 + 31), (1000, 128), jnp.float32)
        _rk = jax.random.fold_in(_tk, 7)
        W_top1 = 0.0441942 * jax.random.normal(jax.random.fold_in(_tk, 801), (512, 512), jnp.float32)
        W_top2 = 0.0441942 * jax.random.normal(jax.random.fold_in(_tk, 802), (512, 256), jnp.float32)
        W_top3 = 0.0625 * jax.random.normal(jax.random.fold_in(_tk, 803), (256, 1), jnp.float32)
        b_top1 = jnp.zeros((512,), jnp.float32)
        b_top2 = jnp.zeros((256,), jnp.float32)
        return (dense_ctx, ids, tbl_0, tbl_1, tbl_2, tbl_3, tbl_4, tbl_5, tbl_6, tbl_7, tbl_8, tbl_9, tbl_10, tbl_11, tbl_12, tbl_13, tbl_14, tbl_15, tbl_16, tbl_17, tbl_18, tbl_19, tbl_20, tbl_21, tbl_22, tbl_23, tbl_24, tbl_25, tbl_26, tbl_27, tbl_28, tbl_29, tbl_30, tbl_31, W_top1, b_top1, W_top2, b_top2, W_top3)
    dense_ctx, ids, tbl_0, tbl_1, tbl_2, tbl_3, tbl_4, tbl_5, tbl_6, tbl_7, tbl_8, tbl_9, tbl_10, tbl_11, tbl_12, tbl_13, tbl_14, tbl_15, tbl_16, tbl_17, tbl_18, tbl_19, tbl_20, tbl_21, tbl_22, tbl_23, tbl_24, tbl_25, tbl_26, tbl_27, tbl_28, tbl_29, tbl_30, tbl_31, W_top1, b_top1, W_top2, b_top2, W_top3 = _rec_inputs()

    def _L0_rec_setup():
        import jax, jax.numpy as jnp
        import numpy as np
        N_FEATS = 32
        EMBED_D = 128
        BATCH = 2048
        SELF_INTERACTION = False
        key = jax.random.key(seed)
        x = jax.random.normal(key, (BATCH, N_FEATS, EMBED_D), dtype=jnp.float32)
        return {'x': x}
    _L0_rec_all = _L0_rec_setup()
    _L0_rec_in = {k: v for k, v in _L0_rec_all.items() if k in ()}
    del _L0_rec_all
    return {'dense_ctx': dense_ctx, 'ids': ids, 'tbl_0': tbl_0, 'tbl_1': tbl_1, 'tbl_2': tbl_2, 'tbl_3': tbl_3, 'tbl_4': tbl_4, 'tbl_5': tbl_5, 'tbl_6': tbl_6, 'tbl_7': tbl_7, 'tbl_8': tbl_8, 'tbl_9': tbl_9, 'tbl_10': tbl_10, 'tbl_11': tbl_11, 'tbl_12': tbl_12, 'tbl_13': tbl_13, 'tbl_14': tbl_14, 'tbl_15': tbl_15, 'tbl_16': tbl_16, 'tbl_17': tbl_17, 'tbl_18': tbl_18, 'tbl_19': tbl_19, 'tbl_20': tbl_20, 'tbl_21': tbl_21, 'tbl_22': tbl_22, 'tbl_23': tbl_23, 'tbl_24': tbl_24, 'tbl_25': tbl_25, 'tbl_26': tbl_26, 'tbl_27': tbl_27, 'tbl_28': tbl_28, 'tbl_29': tbl_29, 'tbl_30': tbl_30, 'tbl_31': tbl_31, 'W_top1': W_top1, 'b_top1': b_top1, 'W_top2': W_top2, 'b_top2': b_top2, 'W_top3': W_top3}

def reference(dense_ctx, ids, tbl_0, tbl_1, tbl_2, tbl_3, tbl_4, tbl_5, tbl_6, tbl_7, tbl_8, tbl_9, tbl_10, tbl_11, tbl_12, tbl_13, tbl_14, tbl_15, tbl_16, tbl_17, tbl_18, tbl_19, tbl_20, tbl_21, tbl_22, tbl_23, tbl_24, tbl_25, tbl_26, tbl_27, tbl_28, tbl_29, tbl_30, tbl_31, W_top1, b_top1, W_top2, b_top2, W_top3):
    import jax
    import jax.numpy as jnp

    def _L0_rec_ref(x):
        import jax, jax.numpy as jnp
        import numpy as np
        N_FEATS = 32
        EMBED_D = 128
        BATCH = 2048
        SELF_INTERACTION = False
        B, N, D = x.shape
        dot = jnp.einsum('bnd,bmd->bnm', x, x)
        k = 0 if SELF_INTERACTION else 1
        iu, ju = jnp.triu_indices(N, k=k)
        flat = dot[:, iu, ju]
        return flat
    e = jnp.stack([tbl_0[ids[:, 0]], tbl_1[ids[:, 1]], tbl_2[ids[:, 2]], tbl_3[ids[:, 3]], tbl_4[ids[:, 4]], tbl_5[ids[:, 5]], tbl_6[ids[:, 6]], tbl_7[ids[:, 7]], tbl_8[ids[:, 8]], tbl_9[ids[:, 9]], tbl_10[ids[:, 10]], tbl_11[ids[:, 11]], tbl_12[ids[:, 12]], tbl_13[ids[:, 13]], tbl_14[ids[:, 14]], tbl_15[ids[:, 15]], tbl_16[ids[:, 16]], tbl_17[ids[:, 17]], tbl_18[ids[:, 18]], tbl_19[ids[:, 19]], tbl_20[ids[:, 20]], tbl_21[ids[:, 21]], tbl_22[ids[:, 22]], tbl_23[ids[:, 23]], tbl_24[ids[:, 24]], tbl_25[ids[:, 25]], tbl_26[ids[:, 26]], tbl_27[ids[:, 27]], tbl_28[ids[:, 28]], tbl_29[ids[:, 29]], tbl_30[ids[:, 30]], tbl_31[ids[:, 31]]], axis=1)
    z = _L0_rec_ref(e)
    z = z.reshape(z.shape[0], -1)
    h = jnp.concatenate([z, dense_ctx], axis=1)
    h = jnp.maximum(h @ W_top1 + b_top1, 0.0)
    h = jnp.maximum(h @ W_top2 + b_top2, 0.0)
    y = h @ W_top3
    return y

_drawn_inputs = setup_inputs


def setup_inputs(seed=0):
    import zlib

    import numpy as np

    out = dict(_drawn_inputs(seed))
    spreads = {'b_top1': (0.0, 0.1), 'b_top2': (0.0, 0.1)}
    factors = {}
    for name, (base, spread) in spreads.items():
        noise = np.random.default_rng([zlib.crc32(name.encode()), seed]).standard_normal(out[name].shape)
        drawn = base * np.exp(spread * noise) if base else spread * noise
        out[name] = jnp.asarray(drawn.astype(out[name].dtype))
    for name, factor in factors.items():
        out[name] = (out[name] * factor).astype(out[name].dtype)
    return out
```

```python
from contextlib import ExitStack

import numpy as np

import concourse.bass as bass
from concourse import mybir

P = 128
F = 32
S = 512
HALF = F // 2
N_SMALL = 8
N_GATHER = F - N_SMALL
GROUP = 16
CHUNKS = GROUP * N_GATHER // P
N_GROUPS = S // GROUP
RING = 18
BATCH = 64
GPB = BATCH // GROUP
N_BATCH = S // BATCH
QUADS = BATCH // 4
BLOCK = 128
N_BLOCK = S // BLOCK
KT = 4
T_SLOTS = 3

ALU = mybir.AluOpType
ACT = mybir.ActivationFunctionType
F32 = mybir.dt.float32
F16 = mybir.dt.float16
I32 = mybir.dt.int32


def small_features(rows):
    return sorted(sorted(range(F), key=lambda f: (rows[f], f))[:N_SMALL])


def build(nc, rows, table, gather_ids, gather_base, small_ids, row_ids, low_mask, dense_mask,
          dense, identity, w1, b1, w2, b2, w3, out):
    small = small_features(rows)
    first_row = [sum(rows[:f]) for f in range(F)]
    H1 = w1.shape[2]
    H2 = w2.shape[2]
    M1, M2 = H1 // P, H2 // P
    RPP = row_ids.shape[1]
    small_parts = [rows[f] // RPP for f in small]

    with ExitStack() as ctx:
        def sb(name, shape, dt=F32):
            return ctx.enter_context(nc.sbuf_tensor(name, shape, dt))

        def psum(name, shape):
            return ctx.enter_context(nc.psum_tensor(name, shape, F32))

        def sem(name):
            return ctx.enter_context(nc.semaphore(name))

        ident = sb("ident", [P, P])
        raw_ids = sb("raw_ids", [P, N_GROUPS * CHUNKS], I32)
        base_ids = sb("base_ids", [P, N_GROUPS * CHUNKS], I32)
        row_of = sb("row_of", [P, N_GROUPS * CHUNKS], I32)
        rows_in = sb("rows_in", [P, RING, CHUNKS, P])
        small_bc = sb("small_bc", [P, N_SMALL, S], I32)
        small_half = sb("small_half", [P, 2, S], F16)
        row_num = sb("row_num", [P, RPP])
        tab = sb("tab", [P, T_SLOTS, RPP, P])
        onehot = sb("onehot", [P, 2, RPP, S])
        et_padded = sb("et_padded", [P, HALF + S * F])
        et = et_padded[:, HALF:].rearrange("p (s f) -> p s f", f=F)
        mask_low = sb("mask_low", [P, 4, KT], I32)
        mask_dense = sb("mask_dense", [P, KT], I32)
        dense_at = sb("dense_at", [P, KT, S])
        z = sb("z", [P, 2, KT, BLOCK])
        w1_sb = sb("w1_sb", [P, KT, H1])
        w2_sb = sb("w2_sb", [P, M1, H2])
        w3_sb = sb("w3_sb", [P, M2])
        b1_sb = sb("b1_sb", [P, M1])
        b2_sb = sb("b2_sb", [P, M2])
        h1 = sb("h1", [P, M1, BLOCK])
        h2 = sb("h2", [P, M2, BLOCK])
        y_sb = sb("y_sb", [1, S])

        turned = psum("turned", [P, 2, 512])
        high = psum("high", [P, QUADS, 4, HALF])
        low = psum("low", [P, QUADS, 4, HALF])
        h1_ps = psum("h1_ps", [P, M1, BLOCK])
        h2y_ps = psum("h2y_ps", [P, 4, BLOCK])
        picked = high[:].rearrange("p (b c) s a -> p b (c s a)", b=2)

        ids_loaded = sem("ids_loaded")
        rows_known = sem("rows_known")
        small_loaded = [sem(f"small_loaded{i}") for i in range(2)]
        consts_loaded = sem("consts_loaded")
        weights_loaded = sem("weights_loaded")
        dense_zeroed = sem("dense_zeroed")
        pad_zeroed = sem("pad_zeroed")
        dense_loaded = sem("dense_loaded")
        tab_loaded = [sem(f"tab_loaded{i}") for i in range(T_SLOTS)]
        gathered = [sem(f"gathered{i}") for i in range(RING)]
        small_halved = sem("small_halved")
        onehot_made = sem("onehot_made")
        small_picked = sem("small_picked")
        small_placed = sem("small_placed")
        transposed = sem("transposed")
        placed_dve = sem("placed_dve")
        placed_act = sem("placed_act")
        products_done = sem("products_done")
        high_copied = sem("high_copied")
        low_copied = sem("low_copied")
        z_ready = sem("z_ready")
        l1_done = sem("l1_done")
        h1_ready = sem("h1_ready")
        l2_done = sem("l2_done")
        h2_ready = sem("h2_ready")
        l3_done = sem("l3_done")
        y_copied = sem("y_copied")
        out_stored = sem("out_stored")

        block = ctx.enter_context(nc.Block())

        @block.sync
        def _(sp):
            sp.dma_start(raw_ids[:], gather_ids).then_inc(ids_loaded, 16)
            sp.dma_start(base_ids[:], gather_base).then_inc(ids_loaded, 16)

            def load_table(i):
                r0 = first_row[small[i]]
                n = small_parts[i]
                sp.dma_start(tab[0:n, i % T_SLOTS],
                             table[r0:r0 + n * RPP, :].rearrange("(p r) d -> p r d", r=RPP)
                             ).then_inc(tab_loaded[i % T_SLOTS], 16)

            load_table(0)
            sp.dma_start(small_bc[:, 1:, :], small_ids[1:, :].partition_broadcast(P)
                         ).then_inc(small_loaded[1], 16)
            for i in range(1, T_SLOTS):
                load_table(i)
            sp.dma_start(ident[:], identity).then_inc(consts_loaded, 16)
            sp.dma_start(mask_low[:], low_mask).then_inc(consts_loaded, 16)
            sp.dma_start(mask_dense[:], dense_mask).then_inc(consts_loaded, 16)
            sp.wait_ge(dense_zeroed, 1)
            for a in range(HALF):
                row = 32 * (a // KT) + HALF + a
                sp.dma_start(dense_at[row:row + 1, a % KT, :], dense[a:a + 1, :]
                             ).then_inc(dense_loaded, 16)
            for i in range(T_SLOTS, N_SMALL):
                sp.wait_ge(small_picked, i - T_SLOTS + 1)
                load_table(i)
            for dst, src in ((w1_sb, w1), (w2_sb, w2), (w3_sb, w3), (b1_sb, b1), (b2_sb, b2)):
                sp.dma_start(dst[:], src).then_inc(weights_loaded, 16)
            sp.wait_ge(y_copied, N_BLOCK)
            sp.dma_start(out, y_sb[:]).then_inc(out_stored, 16)
            sp.wait_ge(out_stored, 16)

        @block.gpsimd
        def _(pool):
            pool.wait_ge(rows_known, 1)
            for g in range(N_GROUPS):
                if g >= RING:
                    pool.wait_ge(transposed, g - RING + 1)
                for c in range(CHUNKS):
                    n = g * CHUNKS + c
                    nc.gpsimd.indirect_dma_start(
                        out=rows_in[:, g % RING, c, :], out_offset=None, in_=table,
                        in_offset=bass.IndirectOffsetOnAxis(ap=row_of[:, n:n + 1], axis=0)
                    ).then_inc(gathered[g % RING], 16)

        def place_group(copy, g):
            return copy(et[:, g * GROUP:(g + 1) * GROUP, 0:N_GATHER],
                        turned[:, g % 2, 0:GROUP * N_GATHER].rearrange("p (s f) -> p s f", s=GROUP))

        def z_block(k, q, s):
            col = (k % 2) * BATCH + s * QUADS
            return z[32 * q:32 * q + 32, (k // 2) % 2, :, col:col + QUADS]

        def product_block(src, q, s):
            return src[32 * s:32 * s + 32, :, s, KT * q:KT * q + KT].rearrange("p c k -> p k c")

        @block.tensor
        def _(pe):
            for i in range(N_SMALL):
                pe.wait_ge(tab_loaded[i % T_SLOTS], 16 * (i // T_SLOTS + 1))
                if i >= 2:
                    pe.wait_ge(small_placed, i - 1)
                n = small_parts[i]
                for r in range(RPP):
                    pe.wait_ge(onehot_made, i * RPP + r + 1)
                    mm = nc.tensor.matmul(picked[:, i % 2, :], tab[0:n, i % T_SLOTS, r, :],
                                          onehot[0:n, i % 2, r, :],
                                          start=(r == 0), stop=(r == RPP - 1))
                mm.then_inc(small_picked, 1)

            def transpose_batch(k):
                for g in range(k * GPB, (k + 1) * GPB):
                    if g == 0:
                        pe.wait_ge(consts_loaded, 48)
                    pe.wait_ge(gathered[g % RING], 16 * CHUNKS * (g // RING + 1))
                    if g >= 2:
                        pe.wait_ge((placed_dve, placed_act)[g % 2], g // 2)
                    for c in range(CHUNKS):
                        mm = nc.tensor.transpose(turned[:, g % 2, c * P:(c + 1) * P],
                                                 rows_in[:, g % RING, c, :], ident[:])
                    mm.then_inc(transposed, 1)

            def products(k):
                if k == 0:
                    pe.wait_ge(small_placed, N_SMALL)
                    pe.wait_ge(pad_zeroed, 1)
                else:
                    pe.wait_ge(z_ready, k)
                for g in range(k * GPB, (k + 1) * GPB):
                    pe.wait_ge((placed_dve, placed_act)[g % 2], g // 2 + 1)
                    for c in range((g % GPB) * 4, (g % GPB) * 4 + 4):
                        s0 = k * BATCH + 4 * c
                        four = et[:, s0:s0 + 4, :]
                        nc.tensor.matmul(high[:, c], four, four[:, :, HALF:F],
                                         start=True, stop=True)
                        mm = nc.tensor.matmul(low[:, c], et_padded[:, s0 * F:(s0 + 4) * F],
                                              four[:, :, 0:HALF], start=True, stop=True)
                mm.then_inc(products_done, 1)

            def layer1(b):
                if b == 0:
                    pe.wait_ge(weights_loaded, 16 * 5)
                pe.wait_ge(z_ready, 2 * (b + 1))
                if b >= 1:
                    pe.wait_ge(h1_ready, M1 * b)
                for m in range(M1):
                    for t in range(KT):
                        mm = nc.tensor.matmul(h1_ps[:, m, :], w1_sb[:, t, m * P:(m + 1) * P],
                                              z[:, b % 2, t, :], start=(t == 0), stop=(t == KT - 1))
                mm.then_inc(l1_done, 1)

            def layers23(b):
                pe.wait_ge(h1_ready, M1 * (b + 1))
                if b >= 1:
                    pe.wait_ge(y_copied, b)
                for m in range(M2):
                    for t in range(M1):
                        mm = nc.tensor.matmul(h2y_ps[:, m, :], w2_sb[:, t, m * P:(m + 1) * P],
                                              h1[:, t, :], start=(t == 0), stop=(t == M1 - 1))
                mm.then_inc(l2_done, 1)
                pe.wait_ge(h2_ready, M2 * (b + 1))
                for t in range(M2):
                    mm = nc.tensor.matmul(h2y_ps[0:1, M2, :], w3_sb[:, t:t + 1], h2[:, t, :],
                                          start=(t == 0), stop=(t == M2 - 1))
                mm.then_inc(l3_done, 1)

            for k in range(N_BATCH):
                transpose_batch(k)
                if k >= 2:
                    if k % 2 == 0:
                        layer1(k // 2 - 1)
                    else:
                        layers23(k // 2 - 1)
                products(k)
            layer1(N_BLOCK - 1)
            layers23(N_BLOCK - 1)

        @block.scalar
        def _(act):
            act.dma_start(small_bc[:, 0:1, :], small_ids[0:1, :].partition_broadcast(P)
                          ).then_inc(small_loaded[0], 16)
            act.dma_start(row_num[:], row_ids).then_inc(small_loaded[0], 16)

            def place_small(i):
                act.wait_ge(small_picked, i + 1)
                nc.scalar.copy(et[:, :, N_GATHER + i], picked[:, i % 2, :]).then_inc(small_placed, 1)

            for i in range(N_SMALL):
                if i == 0:
                    act.wait_ge(small_loaded[0], 32)
                if i == 1:
                    act.wait_ge(small_loaded[1], 16)
                if i >= 2:
                    act.wait_ge(onehot_made, RPP * (i - 1))
                nc.scalar.copy(small_half[:, i % 2, :], small_bc[:, i, :]).then_inc(small_halved, 1)
                if i >= 1:
                    place_small(i - 1)
            place_small(N_SMALL - 1)

            def relu1(b):
                act.wait_ge(l1_done, b + 1)
                if b >= 1:
                    act.wait_ge(l2_done, b)
                if b == 0:
                    act.wait_ge(weights_loaded, 16 * 5)
                for m in range(M1):
                    nc.scalar.activation(h1[:, m, :], h1_ps[:, m, :], ACT.Relu,
                                         bias=b1_sb[:, m:m + 1]).then_inc(h1_ready, 1)

            for k in range(N_BATCH):
                for g in range(k * GPB + 1, (k + 1) * GPB, 2):
                    act.wait_ge(transposed, g + 1)
                    place_group(nc.scalar.copy, g).then_inc(placed_act, 1)
                if k >= 2 and k % 2 == 0:
                    relu1(k // 2 - 1)
                act.wait_ge(products_done, k + 1)
                if k % 2 == 0 and k // 2 >= 2:
                    act.wait_ge(l1_done, k // 2 - 1)
                for s in range(4):
                    for q in range(4):
                        nc.scalar.copy(z_block(k, q, s), product_block(high, q, s)
                                       ).then_inc(high_copied, 1)
            relu1(N_BLOCK - 1)

        @block.vector
        def _(dve):
            nc.vector.memset(dense_at[:], 0.0).then_inc(dense_zeroed, 1)
            nc.vector.memset(et_padded[:, 0:HALF], 0.0).then_inc(pad_zeroed, 1)
            dve.wait_ge(ids_loaded, 32)
            nc.vector.tensor_tensor(row_of[:], raw_ids[:], base_ids[:], ALU.add
                                    ).then_inc(rows_known, 1)
            for i in range(N_SMALL):
                dve.wait_ge(small_halved, i + 1)
                if i >= 2:
                    dve.wait_ge(small_picked, i - 1)
                for r in range(RPP):
                    nc.vector.tensor_scalar(onehot[:, i % 2, r, :], small_half[:, i % 2, :],
                                            row_num[:, r:r + 1], None, ALU.is_equal
                                            ).then_inc(onehot_made, 1)

            def relu2(b):
                dve.wait_ge(l2_done, b + 1)
                if b >= 1:
                    dve.wait_ge(l3_done, b)
                if b == 0:
                    dve.wait_ge(weights_loaded, 16 * 5)
                for m in range(M2):
                    nc.vector.tensor_scalar(h2[:, m, :], h2y_ps[:, m, :], b2_sb[:, m:m + 1], 0.0,
                                            ALU.add, ALU.max).then_inc(h2_ready, 1)
                dve.wait_ge(l3_done, b + 1)
                nc.vector.tensor_copy(y_sb[0:1, b * BLOCK:(b + 1) * BLOCK], h2y_ps[0:1, M2, :]
                                      ).then_inc(y_copied, 1)

            for k in range(N_BATCH):
                for g in range(k * GPB, (k + 1) * GPB, 2):
                    dve.wait_ge(transposed, g + 1)
                    place_group(nc.vector.tensor_copy, g).then_inc(placed_dve, 1)
                if k >= 3 and k % 2 == 1:
                    relu2(k // 2 - 1)
                if k == 0:
                    dve.wait_ge(consts_loaded, 48)
                    dve.wait_ge(dense_loaded, 16 * HALF)
                for s in range(4):
                    dve.wait_ge(high_copied, 16 * k + 4 * (s + 1))
                    for q in range(4):
                        nc.vector.copy_predicated(
                            z_block(k, q, s),
                            mask_low[32 * s:32 * s + 32, q, :].unsqueeze(2)
                            .broadcast_to([32, KT, QUADS]),
                            product_block(low, q, s)).then_inc(low_copied, 1)
                dve.wait_ge(low_copied, 16 * (k + 1))
                half = slice((k % 2) * BATCH, (k % 2 + 1) * BATCH)
                nc.vector.copy_predicated(
                    z[:, (k // 2) % 2, :, half],
                    mask_dense[:].unsqueeze(2).broadcast_to([P, KT, BATCH]),
                    dense_at[:, :, k * BATCH:(k + 1) * BATCH]).then_inc(z_ready, 1)
            relu2(N_BLOCK - 1)


def layout_constants(rows):
    gather_feats = [f for f in range(F) if f not in small_features(rows)]
    order = gather_feats + small_features(rows)
    first_row = np.concatenate([[0], np.cumsum(rows)[:-1]]).astype(np.int32)
    base = np.tile(first_row[gather_feats], S).reshape(N_GROUPS * CHUNKS, P).T
    pair = {}
    n = 0
    for i in range(F):
        for j in range(i + 1, F):
            pair[i, j] = n
            n += 1
    w1_rows = np.zeros((P, KT), np.int64)
    low_mask = np.zeros((P, 4, KT), np.int32)
    dense_mask = np.zeros((P, KT), np.int32)
    for a in range(HALF):
        q, k = a // KT, a % KT
        for r in range(F):
            b = r - HALF
            if b == a:
                w1_rows[32 * q + r, k] = n + a
                dense_mask[32 * q + r, k] = 1
                continue
            lo, hi = (a, b) if b > a else (r, HALF + a)
            f, g = sorted((order[lo], order[hi]))
            w1_rows[32 * q + r, k] = pair[f, g]
            if b > a:
                low_mask[r::32, q, k] = 1
    return gather_feats, base, w1_rows, low_mask, dense_mask


def kernel(**inputs):
    import concourse.bacc as _bacc
    from concourse.bass_utils import run_bass_kernel_spmd as _run

    x = {k: np.asarray(v) for k, v in inputs.items()}
    tables = [x[f"tbl_{f}"] for f in range(F)]
    rows = [t.shape[0] for t in tables]
    small = small_features(rows)
    rpp = -(-max(rows[f] for f in small) // P)
    gather_feats, base, w1_rows, low_mask, dense_mask = layout_constants(rows)
    ids = x["ids"]

    def sample_order(a):
        return a.reshape(*a.shape[:-1], N_BATCH, QUADS, 4).swapaxes(-1, -2).reshape(a.shape)

    def tiles(w):
        return w.reshape(w.shape[0] // P, P, -1).transpose(1, 0, 2)

    arrays = {
        "table": np.concatenate(tables, axis=0),
        "gather_ids": ids[:, gather_feats].reshape(N_GROUPS * CHUNKS, P).T,
        "gather_base": base,
        "small_ids": ids[:, small].T,
        "row_ids": (np.arange(P)[:, None] * rpp + np.arange(rpp)).astype(np.float32),
        "low_mask": low_mask,
        "dense_mask": dense_mask,
        "dense": sample_order(x["dense_ctx"].T),
        "identity": np.eye(P, dtype=np.float32),
        "w1": x["W_top1"][w1_rows],
        "b1": x["b_top1"].reshape(-1, P).T,
        "w2": tiles(x["W_top2"]),
        "b2": x["b_top2"].reshape(-1, P).T,
        "w3": x["W_top3"].reshape(-1, P).T,
    }
    nc = _bacc.Bacc("TRN2", target_bir_lowering=False, num_devices=1)
    args = []
    for name, a in arrays.items():
        a = arrays[name] = np.ascontiguousarray(a)
        args.append(nc.dram_tensor(name, a.shape, mybir.dt.from_np(a.dtype), kind="ExternalInput").ap())
    out = nc.dram_tensor("out", (1, S), F32, kind="ExternalOutput").ap()
    build(nc, rows, *args, out)
    y = _run(nc, [arrays], core_ids=[0]).results[0]["out"]
    return y.reshape(N_BATCH, 4, QUADS).swapaxes(1, 2).reshape(S, 1)
```

```python
from contextlib import ExitStack

import numpy as np

import concourse.bass as bass
from concourse import mybir

P = 128
F = 32
S = 512
HALF = F // 2
N_SMALL = 8
N_GATHER = F - N_SMALL
GROUP = 16
CHUNKS = GROUP * N_GATHER // P
N_GROUPS = S // GROUP
RING = 18
BATCH = 64
GPB = BATCH // GROUP
N_BATCH = S // BATCH
QUADS = BATCH // 4
BLOCK = 128
N_BLOCK = S // BLOCK
KT = 4
T_SLOTS = 3
SHIFT = [(r + HALF) % F for r in range(F)]

ALU = mybir.AluOpType
ACT = mybir.ActivationFunctionType
F32 = mybir.dt.float32
F16 = mybir.dt.float16
BF16 = mybir.dt.bfloat16
I32 = mybir.dt.int32
U16 = mybir.dt.uint16
U8 = mybir.dt.uint8


def small_features(rows):
    return sorted(sorted(range(F), key=lambda f: (rows[f], f))[:N_SMALL])


def build(nc, rows, table, gather_ids, gather_base, small_ids, row_ids, low_mask, dense_mask,
          dense, identity, w1, b1, w2, b2, w3, out):
    small = small_features(rows)
    first_row = [sum(rows[:f]) for f in range(F)]
    H1 = w1.shape[2]
    H2 = w2.shape[2]
    M1, M2 = H1 // P, H2 // P
    RPP = row_ids.shape[1]
    small_parts = [rows[f] // RPP for f in small]

    with ExitStack() as ctx:
        def sb(name, shape, dt=F32):
            return ctx.enter_context(nc.sbuf_tensor(name, shape, dt))

        def psum(name, shape):
            return ctx.enter_context(nc.psum_tensor(name, shape, F32))

        def sem(name):
            return ctx.enter_context(nc.semaphore(name))

        ident = sb("ident", [P, P])
        raw_ids = sb("raw_ids", [P, N_GROUPS * CHUNKS], I32)
        base_ids = sb("base_ids", [P, N_GROUPS * CHUNKS], I32)
        row_of = sb("row_of", [P, N_GROUPS * CHUNKS], I32)
        rows_in = sb("rows_in", [P, RING, CHUNKS, P])
        small_bc = sb("small_bc", [P, N_SMALL, S], I32)
        small_half = sb("small_half", [P, 2, S], F16)
        row_num = sb("row_num", [P, RPP])
        tab = sb("tab", [P, T_SLOTS, RPP, P])
        tab_top = tab[:].rearrange("p b r d -> p b (r d)").bitcast(BF16).rearrange(
            "p b (r d h) -> p b r d h", d=P, h=2)[:, :, :, :, 1]
        tab_byte = tab[:].rearrange("p b r d -> p b (r d)").bitcast(U8).rearrange(
            "p b (w y) -> p b w y", y=4)
        byte1 = sb("byte1", [P, 2, RPP * P], BF16)
        byte0 = sb("byte0", [P, 2, RPP * P], BF16)
        onehot = sb("onehot", [P, 2, RPP, S], BF16)
        et_padded = sb("et_padded", [P, HALF + S * F])
        et = et_padded[:, HALF:].rearrange("p (s f) -> p s f", f=F)
        et_top = et_padded[:, HALF:].bitcast(BF16).rearrange("p (s f h) -> p s f h", f=F, h=2)
        et_low = et_padded[:, HALF:].bitcast(U16).rearrange("p (s f h) -> p s f h", f=F, h=2)
        mask_low = sb("mask_low", [P, HALF], I32)
        mask_dense = sb("mask_dense", [P, KT], I32)
        dense_at = sb("dense_at", [P, KT, S])
        own = sb("own", [P, 2, QUADS, F])
        packed = sb("packed", [P, 2, QUADS, HALF])
        z = sb("z", [P, 2, KT, BLOCK])
        w1_sb = sb("w1_sb", [P, KT, H1])
        w2_sb = sb("w2_sb", [P, M1, H2])
        w3_sb = sb("w3_sb", [P, M2])
        b1_sb = sb("b1_sb", [P, M1])
        b2_sb = sb("b2_sb", [P, M2])
        h1 = sb("h1", [P, M1, BLOCK])
        h2 = sb("h2", [P, M2, BLOCK])
        y_sb = sb("y_sb", [1, S])

        turned = psum("turned", [P, 2, 512])
        dots = psum("dots", [P, QUADS, 4, F])
        h1_ps = psum("h1_ps", [P, M1, BLOCK])
        h2y_ps = psum("h2y_ps", [P, 4, BLOCK])
        picked = dots[:].rearrange("p (b h c) s f -> p b h (c s f)", b=2, h=2)

        ids_loaded = sem("ids_loaded")
        rows_known = sem("rows_known")
        small_loaded = [sem(f"small_loaded{i}") for i in range(2)]
        consts_loaded = sem("consts_loaded")
        weights_loaded = sem("weights_loaded")
        dense_zeroed = sem("dense_zeroed")
        dense_loaded = sem("dense_loaded")
        tab_loaded = [sem(f"tab_loaded{i}") for i in range(T_SLOTS)]
        gathered = [sem(f"gathered{i}") for i in range(RING)]
        small_halved = sem("small_halved")
        onehot_made = sem("onehot_made")
        small_picked = sem("small_picked")
        small_placed = sem("small_placed")
        transposed = sem("transposed")
        placed_dve = sem("placed_dve")
        placed_act = sem("placed_act")
        products_done = sem("products_done")
        bytes_dve = sem("bytes_dve")
        bytes_act = sem("bytes_act")
        own_act = sem("own_act")
        own_dve = sem("own_dve")
        shifted = sem("shifted")
        packed_ready = sem("packed_ready")
        spread_act = sem("spread_act")
        spread_dve = sem("spread_dve")
        z_ready = sem("z_ready")
        l1_done = sem("l1_done")
        h1_ready = sem("h1_ready")
        l2_done = sem("l2_done")
        h2_ready = sem("h2_ready")
        l3_done = sem("l3_done")
        y_copied = sem("y_copied")
        out_stored = sem("out_stored")

        block = ctx.enter_context(nc.Block())

        @block.sync
        def _(sp):
            sp.dma_start(raw_ids[:], gather_ids).then_inc(ids_loaded, 16)
            sp.dma_start(base_ids[:], gather_base).then_inc(ids_loaded, 16)

            def load_table(i):
                r0 = first_row[small[i]]
                n = small_parts[i]
                sp.dma_start(tab[0:n, i % T_SLOTS],
                             table[r0:r0 + n * RPP, :].rearrange("(p r) d -> p r d", r=RPP)
                             ).then_inc(tab_loaded[i % T_SLOTS], 16)

            load_table(0)
            sp.dma_start(small_bc[:, 1:, :], small_ids[1:, :].partition_broadcast(P)
                         ).then_inc(small_loaded[1], 16)
            for i in range(1, T_SLOTS):
                load_table(i)
            sp.dma_start(ident[:], identity).then_inc(consts_loaded, 16)
            sp.dma_start(mask_low[:], low_mask).then_inc(consts_loaded, 16)
            sp.dma_start(mask_dense[:], dense_mask).then_inc(consts_loaded, 16)
            sp.wait_ge(dense_zeroed, 1)
            for a in range(HALF):
                row = 32 * (a // KT) + a
                sp.dma_start(dense_at[row:row + 1, a % KT, :], dense[a:a + 1, :]
                             ).then_inc(dense_loaded, 16)
            for i in range(T_SLOTS, N_SMALL):
                sp.wait_ge(small_picked, i - T_SLOTS + 1)
                load_table(i)
            for dst, src in ((w1_sb, w1), (w2_sb, w2), (w3_sb, w3), (b1_sb, b1), (b2_sb, b2)):
                sp.dma_start(dst[:], src).then_inc(weights_loaded, 16)
            sp.wait_ge(y_copied, N_BLOCK)
            sp.dma_start(out, y_sb[:]).then_inc(out_stored, 16)
            sp.wait_ge(out_stored, 16)

        @block.gpsimd
        def _(pool):
            pool.wait_ge(rows_known, 1)
            for g in range(N_GROUPS):
                if g >= RING:
                    pool.wait_ge(transposed, g - RING + 1)
                for c in range(CHUNKS):
                    n = g * CHUNKS + c
                    nc.gpsimd.indirect_dma_start(
                        out=rows_in[:, g % RING, c, :], out_offset=None, in_=table,
                        in_offset=bass.IndirectOffsetOnAxis(ap=row_of[:, n:n + 1], axis=0)
                    ).then_inc(gathered[g % RING], 16)

        def place_group(copy, g):
            return copy(et[:, g * GROUP:(g + 1) * GROUP, 0:N_GATHER],
                        turned[:, g % 2, 0:GROUP * N_GATHER].rearrange("p (s f) -> p s f", s=GROUP))

        def own_block(copy, k, s):
            return copy(own[32 * s:32 * s + 32, k % 2], dots[32 * s:32 * s + 32, :, s, :])

        def spread(copy, k, q, s):
            col = (k % 2) * BATCH + s * QUADS
            return copy(z[32 * q:32 * q + 32, (k // 2) % 2, :, col:col + QUADS],
                        packed[32 * s:32 * s + 32, k % 2, :, KT * q:KT * q + KT]
                        .rearrange("p c k -> p k c"))

        @block.tensor
        def _(pe):
            for i in range(N_SMALL):
                pe.wait_ge(tab_loaded[i % T_SLOTS], 16 * (i // T_SLOTS + 1))
                if i >= 2:
                    pe.wait_ge(small_placed, 2 * (i - 1))
                n = small_parts[i]
                for r in range(RPP):
                    pe.wait_ge(onehot_made, i * RPP + r + 1)
                    nc.tensor.matmul(picked[:, i % 2, 0, :], tab_top[0:n, i % T_SLOTS, r],
                                     onehot[0:n, i % 2, r, :],
                                     start=(r == 0), stop=(r == RPP - 1))
                pe.wait_ge(bytes_dve, i + 1)
                pe.wait_ge(bytes_act, i + 1)
                for r in range(RPP):
                    for byte in (byte1, byte0):
                        mm = nc.tensor.matmul(picked[:, i % 2, 1, :],
                                              byte[0:n, i % 2, r * P:(r + 1) * P],
                                              onehot[0:n, i % 2, r, :],
                                              start=(r == 0 and byte is byte1),
                                              stop=(r == RPP - 1 and byte is byte0))
                mm.then_inc(small_picked, 1)

            def transpose_batch(k):
                for g in range(k * GPB, (k + 1) * GPB):
                    if g == 0:
                        pe.wait_ge(consts_loaded, 48)
                    pe.wait_ge(gathered[g % RING], 16 * CHUNKS * (g // RING + 1))
                    if g >= 2:
                        pe.wait_ge((placed_dve, placed_act)[g % 2], g // 2)
                    for c in range(CHUNKS):
                        mm = nc.tensor.transpose(turned[:, g % 2, c * P:(c + 1) * P],
                                                 rows_in[:, g % RING, c, :], ident[:])
                    mm.then_inc(transposed, 1)

            def products(k):
                if k == 0:
                    pe.wait_ge(small_placed, 2 * N_SMALL)
                else:
                    pe.wait_ge(own_act, 2 * k)
                    pe.wait_ge(own_dve, 2 * k)
                for g in range(k * GPB, (k + 1) * GPB):
                    pe.wait_ge((placed_dve, placed_act)[g % 2], g // 2 + 1)
                    for c in range((g % GPB) * 4, (g % GPB) * 4 + 4):
                        s0 = k * BATCH + 4 * c
                        four = et_padded[:, HALF + s0 * F:HALF + (s0 + 4) * F]
                        mm = nc.tensor.matmul(dots[:, c], four, four, start=True, stop=True)
                mm.then_inc(products_done, 1)

            def layer1(b, half):
                if half == 0:
                    if b == 0:
                        pe.wait_ge(weights_loaded, 16 * 5)
                    pe.wait_ge(z_ready, 2 * (b + 1))
                    if b >= 1:
                        pe.wait_ge(h1_ready, M1 * b)
                for m in range(half * M1 // 2, (half + 1) * M1 // 2):
                    for t in range(KT):
                        mm = nc.tensor.matmul(h1_ps[:, m, :], w1_sb[:, t, m * P:(m + 1) * P],
                                              z[:, b % 2, t, :], start=(t == 0), stop=(t == KT - 1))
                if half == 1:
                    mm.then_inc(l1_done, 1)

            def layer2(b):
                pe.wait_ge(h1_ready, M1 * (b + 1))
                if b >= 1:
                    pe.wait_ge(y_copied, b)
                for m in range(M2):
                    for t in range(M1):
                        mm = nc.tensor.matmul(h2y_ps[:, m, :], w2_sb[:, t, m * P:(m + 1) * P],
                                              h1[:, t, :], start=(t == 0), stop=(t == M1 - 1))
                mm.then_inc(l2_done, 1)

            def layer3(b):
                pe.wait_ge(h2_ready, M2 * (b + 1))
                for t in range(M2):
                    mm = nc.tensor.matmul(h2y_ps[0:1, M2, :], w3_sb[:, t:t + 1], h2[:, t, :],
                                          start=(t == 0), stop=(t == M2 - 1))
                mm.then_inc(l3_done, 1)

            transpose_batch(0)
            for k in range(N_BATCH):
                products(k)
                b = k // 2 - 1
                if b >= 0:
                    if k % 2 == 0:
                        layer1(b, 0)
                    else:
                        layer2(b)
                if k + 1 < N_BATCH:
                    transpose_batch(k + 1)
                if b >= 0:
                    if k % 2 == 0:
                        layer1(b, 1)
                    else:
                        layer3(b)
            layer1(N_BLOCK - 1, 0)
            layer1(N_BLOCK - 1, 1)
            layer2(N_BLOCK - 1)
            layer3(N_BLOCK - 1)

        @block.scalar
        def _(act):
            act.dma_start(small_bc[:, 0:1, :], small_ids[0:1, :].partition_broadcast(P)
                          ).then_inc(small_loaded[0], 16)
            act.dma_start(row_num[:], row_ids).then_inc(small_loaded[0], 16)

            def place_small(i):
                act.wait_ge(small_picked, i + 1)
                nc.scalar.copy(et_top[:, :, N_GATHER + i, 1], picked[:, i % 2, 0, :]
                               ).then_inc(small_placed, 1)
                nc.scalar.copy(et_low[:, :, N_GATHER + i, 0], picked[:, i % 2, 1, :]
                               ).then_inc(small_placed, 1)

            for i in range(N_SMALL):
                if i == 0:
                    act.wait_ge(small_loaded[0], 32)
                if i == 1:
                    act.wait_ge(small_loaded[1], 16)
                if i >= 2:
                    act.wait_ge(onehot_made, RPP * (i - 1))
                nc.scalar.copy(small_half[:, i % 2, :], small_bc[:, i, :]).then_inc(small_halved, 1)
                act.wait_ge(tab_loaded[i % T_SLOTS], 16 * (i // T_SLOTS + 1))
                if i >= 2:
                    act.wait_ge(small_picked, i - 1)
                nc.scalar.mul(byte1[0:small_parts[i], i % 2, :], tab_byte[0:small_parts[i], i % T_SLOTS, :, 1], 256.0
                              ).then_inc(bytes_act, 1)
                if i >= 1:
                    place_small(i - 1)
            place_small(N_SMALL - 1)

            def place(k):
                for g in range(k * GPB + 1, (k + 1) * GPB, 2):
                    act.wait_ge(transposed, g + 1)
                    place_group(nc.scalar.copy, g).then_inc(placed_act, 1)

            def relu1(b):
                if b == 0:
                    act.wait_ge(weights_loaded, 16 * 5)
                act.wait_ge(l1_done, b + 1)
                if b >= 1:
                    act.wait_ge(l2_done, b)
                for m in range(M1):
                    nc.scalar.activation(h1[:, m, :], h1_ps[:, m, :], ACT.Relu,
                                         bias=b1_sb[:, m:m + 1]).then_inc(h1_ready, 1)

            def take_own(k):
                act.wait_ge(products_done, k + 1)
                if k >= 2:
                    act.wait_ge(packed_ready, k - 1)
                for s in (0, 1):
                    own_block(nc.scalar.copy, k, s).then_inc(own_act, 1)

            def spread_half(k):
                act.wait_ge(packed_ready, k + 1)
                if k % 2 == 0 and k // 2 >= 2:
                    act.wait_ge(l1_done, k // 2 - 1)
                for s in (0, 1):
                    for q in range(4):
                        spread(nc.scalar.copy, k, q, s).then_inc(spread_act, 1)

            place(0)
            for k in range(N_BATCH):
                take_own(k)
                if k + 2 < N_BATCH:
                    place(k + 1)
                spread_half(k)
                if k + 2 == N_BATCH:
                    place(k + 1)
                if k >= 2 and k % 2 == 0:
                    relu1(k // 2 - 1)
            relu1(N_BLOCK - 1)

        @block.vector
        def _(dve):
            nc.vector.memset(dense_at[:], 0.0).then_inc(dense_zeroed, 1)
            dve.wait_ge(ids_loaded, 32)
            nc.vector.tensor_tensor(row_of[:], raw_ids[:], base_ids[:], ALU.add
                                    ).then_inc(rows_known, 1)
            for i in range(N_SMALL):
                dve.wait_ge(small_halved, i + 1)
                if i >= 2:
                    dve.wait_ge(small_picked, i - 1)
                for r in range(RPP):
                    nc.vector.tensor_scalar(onehot[:, i % 2, r, :], small_half[:, i % 2, :],
                                            row_num[:, r:r + 1], None, ALU.is_equal
                                            ).then_inc(onehot_made, 1)
                dve.wait_ge(tab_loaded[i % T_SLOTS], 16 * (i // T_SLOTS + 1))
                nc.vector.tensor_copy(byte0[0:small_parts[i], i % 2, :], tab_byte[0:small_parts[i], i % T_SLOTS, :, 0]
                                      ).then_inc(bytes_dve, 1)

            def place(k):
                for g in range(k * GPB, (k + 1) * GPB, 2):
                    dve.wait_ge(transposed, g + 1)
                    place_group(nc.vector.tensor_copy, g).then_inc(placed_dve, 1)

            def relu2(b):
                dve.wait_ge(l2_done, b + 1)
                if b >= 1:
                    dve.wait_ge(l3_done, b)
                for m in range(M2):
                    nc.vector.tensor_scalar(h2[:, m, :], h2y_ps[:, m, :], b2_sb[:, m:m + 1], 0.0,
                                            ALU.add, ALU.max).then_inc(h2_ready, 1)

            def keep_y(b):
                dve.wait_ge(l3_done, b + 1)
                nc.vector.tensor_copy(y_sb[0:1, b * BLOCK:(b + 1) * BLOCK], h2y_ps[0:1, M2, :]
                                      ).then_inc(y_copied, 1)

            def take_own(k):
                dve.wait_ge(products_done, k + 1)
                for s in (2, 3):
                    own_block(nc.vector.tensor_copy, k, s).then_inc(own_dve, 1)

            def pack(k):
                dve.wait_ge(own_act, 2 * (k + 1))
                dve.wait_ge(own_dve, 2 * (k + 1))
                if k >= 2:
                    dve.wait_ge(spread_act, 8 * (k - 1))
                    dve.wait_ge(spread_dve, 8 * (k - 1))
                nc.vector.stream_shuffle(packed[:, k % 2], own[:, k % 2, :, HALF:F], SHIFT
                                         ).then_inc(shifted, 1)
                dve.wait_ge(shifted, k + 1)
                nc.vector.copy_predicated(packed[:, k % 2],
                                          mask_low[:].unsqueeze(1).broadcast_to([P, QUADS, HALF]),
                                          own[:, k % 2, :, 0:HALF]).then_inc(packed_ready, 1)

            def spread_half(k):
                dve.wait_ge(packed_ready, k + 1)
                if k % 2 == 0 and k // 2 >= 2:
                    dve.wait_ge(l1_done, k // 2 - 1)
                for s in (2, 3):
                    for q in range(4):
                        spread(nc.vector.tensor_copy, k, q, s).then_inc(spread_dve, 1)
                dve.wait_ge(spread_act, 8 * (k + 1))
                dve.wait_ge(spread_dve, 8 * (k + 1))
                half = slice((k % 2) * BATCH, (k % 2 + 1) * BATCH)
                nc.vector.copy_predicated(
                    z[:, (k // 2) % 2, :, half],
                    mask_dense[:].unsqueeze(2).broadcast_to([P, KT, BATCH]),
                    dense_at[:, :, k * BATCH:(k + 1) * BATCH]).then_inc(z_ready, 1)

            place(0)
            dve.wait_ge(consts_loaded, 48)
            dve.wait_ge(dense_loaded, 16 * HALF)
            dve.wait_ge(weights_loaded, 16 * 5)
            for k in range(N_BATCH):
                b = k // 2 - 1
                take_own(k)
                if b >= 0 and k % 2 == 1:
                    relu2(b)
                pack(k)
                if k + 2 < N_BATCH:
                    place(k + 1)
                spread_half(k)
                if k + 2 == N_BATCH:
                    place(k + 1)
                if b >= 0 and k % 2 == 1:
                    keep_y(b)
            relu2(N_BLOCK - 1)
            keep_y(N_BLOCK - 1)


def layout_constants(rows):
    gather_feats = [f for f in range(F) if f not in small_features(rows)]
    order = gather_feats + small_features(rows)
    first_row = np.concatenate([[0], np.cumsum(rows)[:-1]]).astype(np.int32)
    base = np.tile(first_row[gather_feats], S).reshape(N_GROUPS * CHUNKS, P).T
    pair = {}
    n = 0
    for i in range(F):
        for j in range(i + 1, F):
            pair[i, j] = n
            n += 1
    w1_rows = np.zeros((P, KT), np.int64)
    low_mask = np.zeros((P, HALF), np.int32)
    dense_mask = np.zeros((P, KT), np.int32)
    for a in range(HALF):
        q, k = a // KT, a % KT
        for r in range(F):
            if r == a:
                w1_rows[32 * q + r, k] = n + a
                dense_mask[32 * q + r, k] = 1
                continue
            lo, hi = (HALF + a, HALF + r) if r < a else (a, r)
            f, g = sorted((order[lo], order[hi]))
            w1_rows[32 * q + r, k] = pair[f, g]
            if r > a:
                low_mask[r::32, a] = 1
    return gather_feats, base, w1_rows, low_mask, dense_mask


def kernel(**inputs):
    import concourse.bacc as _bacc
    from concourse.bass_utils import run_bass_kernel_spmd as _run

    x = {k: np.asarray(v) for k, v in inputs.items()}
    tables = [x[f"tbl_{f}"] for f in range(F)]
    rows = [t.shape[0] for t in tables]
    small = small_features(rows)
    rpp = -(-max(rows[f] for f in small) // P)
    gather_feats, base, w1_rows, low_mask, dense_mask = layout_constants(rows)
    ids = x["ids"]

    def sample_order(a):
        return a.reshape(*a.shape[:-1], N_BATCH, QUADS, 4).swapaxes(-1, -2).reshape(a.shape)

    def tiles(w):
        return w.reshape(w.shape[0] // P, P, -1).transpose(1, 0, 2)

    arrays = {
        "table": np.concatenate(tables, axis=0),
        "gather_ids": ids[:, gather_feats].reshape(N_GROUPS * CHUNKS, P).T,
        "gather_base": base,
        "small_ids": ids[:, small].T,
        "row_ids": (np.arange(P)[:, None] * rpp + np.arange(rpp)).astype(np.float32),
        "low_mask": low_mask,
        "dense_mask": dense_mask,
        "dense": sample_order(x["dense_ctx"].T),
        "identity": np.eye(P, dtype=np.float32),
        "w1": x["W_top1"][w1_rows],
        "b1": x["b_top1"].reshape(-1, P).T,
        "w2": tiles(x["W_top2"]),
        "b2": x["b_top2"].reshape(-1, P).T,
        "w3": x["W_top3"].reshape(-1, P).T,
    }
    nc = _bacc.Bacc("TRN2", target_bir_lowering=False, num_devices=1)
    args = []
    for name, a in arrays.items():
        a = arrays[name] = np.ascontiguousarray(a)
        args.append(nc.dram_tensor(name, a.shape, mybir.dt.from_np(a.dtype), kind="ExternalInput").ap())
    out = nc.dram_tensor("out", (1, S), F32, kind="ExternalOutput").ap()
    build(nc, rows, *args, out)
    y = _run(nc, [arrays], core_ids=[0]).results[0]["out"]
    return y.reshape(N_BATCH, 4, QUADS).swapaxes(1, 2).reshape(S, 1)
```

```python
from contextlib import ExitStack

import numpy as np

import concourse.bass as bass
from concourse import mybir

P = 128
F = 32
S = 512
HALF = F // 2
N_SMALL = 8
N_GATHER = F - N_SMALL
GROUP = 16
CHUNKS = GROUP * N_GATHER // P
N_GROUPS = S // GROUP
RING = 18
BATCH = 64
GPB = BATCH // GROUP
N_BATCH = S // BATCH
QUADS = BATCH // 4
BLOCK = 128
N_BLOCK = S // BLOCK
LAST = N_BLOCK - 1
N_EVEN = N_BATCH - 3
SPREAD = [(s, q) for s in range(4) for q in range(4)]
SPREAD_ACT, SPREAD_DVE = SPREAD[:6], SPREAD[6:]
N_WARM = 10
EARLY = N_SMALL - GPB
KT = 4
T_SLOTS = 3
SHIFT = [(r + HALF) % F for r in range(F)]

ALU = mybir.AluOpType
ACT = mybir.ActivationFunctionType
F32 = mybir.dt.float32
F16 = mybir.dt.float16
BF16 = mybir.dt.bfloat16
I32 = mybir.dt.int32
U16 = mybir.dt.uint16
U8 = mybir.dt.uint8


def small_features(rows):
    return sorted(sorted(range(F), key=lambda f: (rows[f], f))[:N_SMALL])


def build(nc, rows, table, gather_ids, small_ids, low_mask, dense_mask,
          dense, identity, w1, b1, w2, b2, w3, out):
    small = small_features(rows)
    first_row = [sum(rows[:f]) for f in range(F)]
    H1 = w1.shape[2]
    H2 = w2.shape[2]
    M1, M2 = H1 // P, H2 // P
    RPP = -(-max(rows[f] for f in small) // P)
    assert all(rows[f] % RPP == 0 and rows[f] <= 2048 for f in small)
    small_parts = [rows[f] // RPP for f in small]

    with ExitStack() as ctx:
        def sb(name, shape, dt=F32):
            return ctx.enter_context(nc.sbuf_tensor(name, shape, dt))

        def psum(name, shape):
            return ctx.enter_context(nc.psum_tensor(name, shape, F32))

        def sem(name):
            return ctx.enter_context(nc.semaphore(name))

        ident = sb("ident", [P, P], BF16)
        id_and_base = sb("id_and_base", [P, 2, N_GROUPS * CHUNKS], I32)
        row_of = sb("row_of", [P, N_GROUPS * CHUNKS], I32)
        rows_in = sb("rows_in", [P, RING, CHUNKS, P])
        rows_half = rows_in[:].rearrange("p g c d -> p (g c d)").bitcast(BF16).rearrange(
            "p (g c d h) -> p g c h d", g=RING, c=CHUNKS, h=2)
        small_bc = sb("small_bc", [P, N_SMALL, S], I32)
        small_half = sb("small_half", [P, 2, S], F16)
        row_num = sb("row_num", [P, RPP])
        warm = sb("warm", [P, S], BF16)
        tab = sb("tab", [P, T_SLOTS, RPP, P])
        tab_top = tab[:].rearrange("p b r d -> p b (r d)").bitcast(BF16).rearrange(
            "p b (r d h) -> p b r d h", d=P, h=2)[:, :, :, :, 1]
        tab_byte = tab[:].rearrange("p b r d -> p b (r d)").bitcast(U8).rearrange(
            "p b (w y) -> p b w y", y=4)
        byte1 = sb("byte1", [P, 2, RPP * P], BF16)
        byte0 = sb("byte0", [P, 2, RPP * P], BF16)
        onehot = sb("onehot", [P, 2, RPP, S], BF16)
        emb = sb("emb", [P, S * F])
        emb_top = emb[:].bitcast(BF16).rearrange("p (s f h) -> p s f h", f=F, h=2)
        emb_halves = emb[:].bitcast(U16).rearrange("p (s w) -> p s w", w=2 * F)
        emb_low = emb[:].bitcast(U16).rearrange("p (s f h) -> p s f h", f=F, h=2)
        mask_low = sb("mask_low", [P, HALF], I32)
        mask_dense = sb("mask_dense", [P, KT], I32)
        dense_at = sb("dense_at", [P, KT, S])
        own = sb("own", [P, 2, QUADS, F])
        packed = sb("packed", [P, 2, QUADS, HALF])
        z = sb("z", [P, 2, KT, BLOCK])
        w1_sb = sb("w1_sb", [P, KT, H1])
        w2_sb = sb("w2_sb", [P, M1, H2])
        w3_sb = sb("w3_sb", [P, M2])
        b1_sb = sb("b1_sb", [P, M1])
        b2_sb = sb("b2_sb", [P, M2])
        h1 = sb("h1", [P, M1, BLOCK])
        h2 = sb("h2", [P, M2, BLOCK])
        y_sb = sb("y_sb", [1, S])

        turned_ps = psum("turned_ps", [P, 2, 512])
        turned = turned_ps[:].rearrange("p b w -> p (b w)").bitcast(BF16).rearrange(
            "p (b h n) -> p b h n", b=2, h=2)[:, :, :, 0:GROUP * N_GATHER]
        dots = psum("dots", [P, QUADS, 4, F])
        h1_ps = psum("h1_ps", [P, M1, BLOCK])
        h2y_ps = psum("h2y_ps", [P, 4, BLOCK])
        last_h1 = dots[:].rearrange("p (m c) s f -> p m (c s f)", m=M1)
        picked = dots[:].rearrange("p (b h c) s f -> p b h (c s f)", b=2, h=2)

        ids_loaded = sem("ids_loaded")
        rows_known = sem("rows_known")
        rows_numbered = sem("rows_numbered")
        warm_zeroed = sem("warm_zeroed")
        small_loaded = [sem(f"small_loaded{i}") for i in range(3)]
        consts_loaded = sem("consts_loaded")
        weights_loaded = sem("weights_loaded")
        dense_zeroed = sem("dense_zeroed")
        dense_loaded = sem("dense_loaded")
        tab_loaded = [sem(f"tab_loaded{i}") for i in range(T_SLOTS)]
        gathered = [sem(f"gathered{i}") for i in range(RING)]
        small_halved = sem("small_halved")
        onehot_made = sem("onehot_made")
        small_picked = sem("small_picked")
        top_placed = sem("top_placed")
        low_placed = sem("low_placed")
        transposed = sem("transposed")
        placed_dve = sem("placed_dve")
        placed_act = sem("placed_act")
        products_done = sem("products_done")
        bytes_dve = sem("bytes_dve")
        bytes_act = sem("bytes_act")
        own_act = sem("own_act")
        own_dve = sem("own_dve")
        shifted = sem("shifted")
        packed_ready = sem("packed_ready")
        spread_act = sem("spread_act")
        spread_dve = sem("spread_dve")
        z_ready = sem("z_ready")
        l1_done = sem("l1_done")
        h1_ready = sem("h1_ready")
        l2_done = sem("l2_done")
        h2_dve = sem("h2_dve")
        h2_act = sem("h2_act")
        l3_done = sem("l3_done")
        y_copied = sem("y_copied")
        out_stored = sem("out_stored")

        block = ctx.enter_context(nc.Block())

        @block.sync
        def _(sp):
            sp.dma_start(id_and_base[:], gather_ids).then_inc(ids_loaded, 16)

            def load_table(i):
                r0 = first_row[small[i]]
                n = small_parts[i]
                sp.dma_start(tab[0:n, i % T_SLOTS],
                             table[r0:r0 + n * RPP, :].rearrange("(p r) d -> p r d", r=RPP)
                             ).then_inc(tab_loaded[i % T_SLOTS], 16)

            load_table(0)
            sp.dma_start(small_bc[:, 1:2, :], small_ids[1:2, :].partition_broadcast(P)
                         ).then_inc(small_loaded[1], 16)
            load_table(1)
            sp.dma_start(small_bc[:, 2:, :], small_ids[2:, :].partition_broadcast(P)
                         ).then_inc(small_loaded[2], 16)
            load_table(2)
            sp.dma_start(ident[:], identity).then_inc(consts_loaded, 16)
            sp.dma_start(mask_low[:], low_mask).then_inc(consts_loaded, 16)
            sp.dma_start(mask_dense[:], dense_mask).then_inc(consts_loaded, 16)
            sp.wait_ge(dense_zeroed, 1)
            for a in range(HALF):
                row = 32 * (a // KT) + a
                sp.dma_start(dense_at[row:row + 1, a % KT, :], dense[a:a + 1, :]
                             ).then_inc(dense_loaded, 16)
            for i in range(T_SLOTS, N_SMALL):
                sp.wait_ge(small_picked, i - T_SLOTS + 1)
                load_table(i)
            for dst, src in ((w1_sb, w1), (w2_sb, w2), (w3_sb, w3), (b1_sb, b1), (b2_sb, b2)):
                sp.dma_start(dst[:], src).then_inc(weights_loaded, 16)
            sp.wait_ge(y_copied, N_BLOCK)
            sp.dma_start(out, y_sb[:]).then_inc(out_stored, 16)
            sp.wait_ge(out_stored, 16)

        @block.gpsimd
        def _(pool):
            nc.gpsimd.iota(row_num[:], [[1, RPP]], base=0, channel_multiplier=RPP,
                           allow_small_or_imprecise_dtypes=True).then_inc(rows_numbered, 1)
            nc.gpsimd.memset(dense_at[:], 0.0).then_inc(dense_zeroed, 1)
            pool.wait_ge(rows_known, 1)
            for g in range(N_GROUPS):
                if g >= RING:
                    pool.wait_ge(transposed, g - RING + 1)
                for c in range(CHUNKS):
                    n = g * CHUNKS + c
                    nc.gpsimd.indirect_dma_start(
                        out=rows_in[:, g % RING, c, :], out_offset=None, in_=table,
                        in_offset=bass.IndirectOffsetOnAxis(ap=row_of[:, n:n + 1], axis=0)
                    ).then_inc(gathered[g % RING], 16)

        def place_group(copy, g):
            return copy(
                emb_halves[:, g * GROUP:(g + 1) * GROUP, 0:2 * N_GATHER].rearrange(
                    "p s (f h) -> p s f h", h=2),
                turned[:, g % 2].rearrange("p h (s f) -> p s f h", s=GROUP).bitcast(U16))

        def groups(k):
            return range(k * GPB, (k + 1) * GPB)

        def h2_tile(b, m):
            return h2y_ps[:, m, :] if b < LAST else (turned_ps[:, 0, 0:BLOCK], h1_ps[:, 0, :])[m]

        def own_block(copy, k, half, s):
            c = slice(half * QUADS // 2, (half + 1) * QUADS // 2)
            return copy(own[32 * s:32 * s + 32, k % 2, c], dots[32 * s:32 * s + 32, c, s, :])

        def spread(copy, k, c, q, s):
            col = (k % 2) * BATCH + s * QUADS
            return copy(z[32 * q:32 * q + 32, (k // 2) % 2, :, col + c.start:col + c.stop],
                        packed[32 * s:32 * s + 32, k % 2, c, KT * q:KT * q + KT]
                        .rearrange("p c k -> p k c"))

        WHOLE = slice(0, QUADS)
        HALVES = [slice(0, QUADS // 2), slice(QUADS // 2, QUADS)]

        @block.tensor
        def _(pe):
            def transpose_group(g):
                if g == 0:
                    pe.wait_ge(consts_loaded, 48)
                pe.wait_ge(gathered[g % RING], 16 * CHUNKS * (g // RING + 1))
                if g >= 2:
                    pe.wait_ge((placed_dve, placed_act)[g % 2], g // 2)
                for c in range(CHUNKS):
                    for h in range(2):
                        mm = nc.tensor.transpose(turned[:, g % 2, h, c * P:(c + 1) * P],
                                                 rows_half[:, g % RING, c, h], ident[:])
                mm.then_inc(transposed, 1)

            pe.wait_ge(warm_zeroed, 1)
            for _ in range(N_WARM):
                nc.tensor.matmul(h1_ps[:].rearrange("p m n -> p (m n)"), warm[:, 0:P], warm[:],
                                 start=True, stop=True)

            for i in range(N_SMALL):
                pe.wait_ge(tab_loaded[i % T_SLOTS], 16 * (i // T_SLOTS + 1))
                if i >= 2:
                    pe.wait_ge(top_placed, i - 1)
                    pe.wait_ge(low_placed, i - 1)
                n = small_parts[i]
                for r in range(RPP):
                    pe.wait_ge(onehot_made, i * RPP + r + 1)
                    nc.tensor.matmul(picked[:, i % 2, 0, :], tab_top[0:n, i % T_SLOTS, r],
                                     onehot[0:n, i % 2, r, :],
                                     start=(r == 0), stop=(r == RPP - 1))
                pe.wait_ge(bytes_dve, i + 1)
                pe.wait_ge(bytes_act, i + 1)
                for r in range(RPP):
                    for byte in (byte1, byte0):
                        mm = nc.tensor.matmul(picked[:, i % 2, 1, :],
                                              byte[0:n, i % 2, r * P:(r + 1) * P],
                                              onehot[0:n, i % 2, r, :],
                                              start=(r == 0 and byte is byte1),
                                              stop=(r == RPP - 1 and byte is byte0))
                mm.then_inc(small_picked, 1)
                if i >= EARLY:
                    transpose_group(i - EARLY)

            def group_products(g):
                k = g // GPB
                if g == 0:
                    pe.wait_ge(top_placed, N_SMALL)
                    pe.wait_ge(low_placed, N_SMALL)
                elif g >= GPB and g % 2 == 0:
                    pe.wait_ge(own_act, g - GPB + 2)
                    pe.wait_ge(own_dve, g - GPB + 2)
                pe.wait_ge((placed_dve, placed_act)[g % 2], g // 2 + 1)
                for c in range((g % GPB) * 4, (g % GPB) * 4 + 4):
                    s0 = k * BATCH + 4 * c
                    four = emb[:, s0 * F:(s0 + 4) * F]
                    mm = nc.tensor.matmul(dots[:, c], four, four, start=True, stop=True)
                if g % 2 == 1:
                    mm.then_inc(products_done, 1)

            def layer1(b):
                if b == 0:
                    pe.wait_ge(weights_loaded, 16 * 5)
                pe.wait_ge(z_ready, 2 * (b + 1))
                if 0 < b < LAST:
                    pe.wait_ge(h1_ready, M1 * b)
                for m in range(M1):
                    tile = h1_ps[:, m, :] if b < LAST else last_h1[:, m, 0:BLOCK]
                    for t in range(KT):
                        mm = nc.tensor.matmul(tile, w1_sb[:, t, m * P:(m + 1) * P],
                                              z[:, b % 2, t, :], start=(t == 0), stop=(t == KT - 1))
                    mm.then_inc(l1_done, 1)

            def layer2(b):
                if 1 <= b < LAST:
                    pe.wait_ge(y_copied, b)
                if b < LAST:
                    pe.wait_ge(h1_ready, M1 * (b + 1))
                    steps = [(m, t) for m in range(M2) for t in range(M1)]
                else:
                    steps = [(m, t) for t in range(M1) for m in range(M2)]
                for n, (m, t) in enumerate(steps):
                    if b == LAST:
                        pe.wait_ge(h1_ready, M1 * b + t + 1)
                    mm = nc.tensor.matmul(h2_tile(b, m), w2_sb[:, t, m * P:(m + 1) * P],
                                          h1[:, t, :], start=(t == 0), stop=(t == M1 - 1))
                mm.then_inc(l2_done, 1)

            def layer3(b):
                pe.wait_ge(h2_dve, (M2 * b + M2) if b < LAST else M2 * b + 1)
                if b == LAST:
                    pe.wait_ge(h2_act, 1)
                    pe.wait_ge(y_copied, b)
                for t in range(M2):
                    mm = nc.tensor.matmul(h2y_ps[0:1, M2, :], w3_sb[:, t:t + 1], h2[:, t, :],
                                          start=(t == 0), stop=(t == M2 - 1))
                mm.then_inc(l3_done, 1)

            for k in range(N_EVEN):
                b = k // 2 - 1
                for i, g in enumerate(groups(k)):
                    group_products(g)
                    transpose_group(g + GPB)
                    if i == 0 and k % 2 == 0 and b >= 1:
                        layer3(b - 1)
                if b >= 0 and k % 2 == 0:
                    layer1(b)
                if b >= 0 and k % 2 == 1:
                    layer2(b)
            g5, g6, g7 = groups(N_EVEN), groups(N_EVEN + 1), groups(N_EVEN + 2)
            transpose_group(g6[0])
            group_products(g5[0])
            transpose_group(g6[1])
            group_products(g5[1])
            group_products(g5[2])
            group_products(g5[3])
            transpose_group(g6[2])
            layer2(LAST - 2)
            group_products(g6[0])
            transpose_group(g6[3])
            layer3(LAST - 2)
            group_products(g6[1])
            group_products(g6[2])
            group_products(g6[3])
            transpose_group(g7[0])
            layer1(LAST - 1)
            transpose_group(g7[1])
            group_products(g7[0])
            transpose_group(g7[2])
            group_products(g7[1])
            group_products(g7[2])
            transpose_group(g7[3])
            group_products(g7[3])
            layer2(LAST - 1)
            layer1(LAST)
            layer3(LAST - 1)
            layer2(LAST)
            layer3(LAST)

        @block.scalar
        def _(act):
            act.dma_start(small_bc[:, 0:1, :], small_ids[0:1, :].partition_broadcast(P)
                          ).then_inc(small_loaded[0], 16)

            def place_small(i):
                act.wait_ge(small_picked, i + 1)
                nc.scalar.copy(emb_low[:, :, N_GATHER + i, 0], picked[:, i % 2, 1, :]
                               ).then_inc(low_placed, 1)

            def place(g):
                act.wait_ge(transposed, g + 1)
                place_group(nc.scalar.copy, g).then_inc(placed_act, 1)

            for i in range(N_SMALL):
                if i < 3:
                    act.wait_ge(small_loaded[i], 16)
                if i >= 2:
                    act.wait_ge(onehot_made, RPP * (i - 1))
                nc.scalar.copy(small_half[:, i % 2, :], small_bc[:, i, :]).then_inc(small_halved, 1)
                act.wait_ge(tab_loaded[i % T_SLOTS], 16 * (i // T_SLOTS + 1))
                if i >= 2:
                    act.wait_ge(small_picked, i - 1)
                n = small_parts[i]
                nc.scalar.mul(byte1[0:n, i % 2, :], tab_byte[0:n, i % T_SLOTS, :, 1], 256.0
                              ).then_inc(bytes_act, 1)
                if i >= 1:
                    place_small(i - 1)
                if i > EARLY and (i - 1 - EARLY) % 2 == 1:
                    place(i - 1 - EARLY)
            place_small(N_SMALL - 1)
            place(GPB - 1)

            def relu1(b):
                if b == 0:
                    act.wait_ge(weights_loaded, 16 * 5)
                if b >= 1:
                    act.wait_ge(l2_done, b)
                for m in range(M1):
                    act.wait_ge(l1_done, M1 * (b + 1) if b < LAST else M1 * b + m + 1)
                    tile = h1_ps[:, m, :] if b < LAST else last_h1[:, m, 0:BLOCK]
                    nc.scalar.activation(h1[:, m, :], tile, ACT.Relu,
                                         bias=b1_sb[:, m:m + 1]).then_inc(h1_ready, 1)

            def take_own(k, half):
                act.wait_ge(products_done, 2 * k + half + 1)
                if k >= 2:
                    act.wait_ge(packed_ready, k - 1)
                for s in (0, 1):
                    own_block(nc.scalar.copy, k, half, s).then_inc(own_act, 1)

            def spread_some(n, k, c):
                act.wait_ge(packed_ready, n + 1)
                if k % 2 == 0 and k // 2 >= 2:
                    act.wait_ge(l1_done, M1 * (k // 2 - 1))
                for s, q in SPREAD_ACT:
                    spread(nc.scalar.copy, k, c, q, s).then_inc(spread_act, 1)

            for k in range(N_EVEN):
                take_own(k, 0)
                place(groups(k + 1)[1])
                take_own(k, 1)
                place(groups(k + 1)[3])
                spread_some(k, k, WHOLE)
                if k >= 2 and k % 2 == 0:
                    relu1(k // 2 - 1)
            k5, k6, k7 = range(N_EVEN, N_BATCH)
            place(groups(k6)[1])
            take_own(k5, 0)
            take_own(k5, 1)
            spread_some(k5, k5, WHOLE)
            place(groups(k6)[3])
            take_own(k6, 0)
            take_own(k6, 1)
            spread_some(k6, k6, WHOLE)
            relu1(LAST - 1)
            place(groups(k7)[1])
            take_own(k7, 0)
            place(groups(k7)[3])
            spread_some(k7, k7, HALVES[0])
            take_own(k7, 1)
            spread_some(k7 + 1, k7, HALVES[1])
            relu1(LAST)
            act.wait_ge(l2_done, LAST + 1)
            nc.scalar.activation(h2[:, 1, :], h2_tile(LAST, 1), ACT.Relu, bias=b2_sb[:, 1:2]
                                 ).then_inc(h2_act, 1)

        @block.vector
        def _(dve):
            nc.vector.memset(warm[:], 0.0).then_inc(warm_zeroed, 1)
            dve.wait_ge(ids_loaded, 16)
            nc.vector.tensor_tensor(row_of[:], id_and_base[:, 0, :], id_and_base[:, 1, :], ALU.add
                                    ).then_inc(rows_known, 1)
            dve.wait_ge(rows_numbered, 1)

            def place(g):
                dve.wait_ge(transposed, g + 1)
                place_group(nc.vector.tensor_copy, g).then_inc(placed_dve, 1)

            def place_small(i):
                dve.wait_ge(small_picked, i + 1)
                nc.vector.tensor_copy(emb_top[:, :, N_GATHER + i, 1], picked[:, i % 2, 0, :]
                                      ).then_inc(top_placed, 1)

            for i in range(N_SMALL):
                dve.wait_ge(small_halved, i + 1)
                if i >= 2:
                    dve.wait_ge(small_picked, i - 1)
                for r in range(RPP):
                    nc.vector.tensor_scalar(onehot[:, i % 2, r, :], small_half[:, i % 2, :],
                                            row_num[:, r:r + 1], None, ALU.is_equal
                                            ).then_inc(onehot_made, 1)
                dve.wait_ge(tab_loaded[i % T_SLOTS], 16 * (i // T_SLOTS + 1))
                n = small_parts[i]
                nc.vector.tensor_copy(byte0[0:n, i % 2, :], tab_byte[0:n, i % T_SLOTS, :, 0]
                                      ).then_inc(bytes_dve, 1)
                if i >= 1:
                    place_small(i - 1)
                if i > EARLY and (i - 1 - EARLY) % 2 == 0:
                    place(i - 1 - EARLY)

            def relu2(b):
                dve.wait_ge(l2_done, b + 1)
                if b >= 1:
                    dve.wait_ge(l3_done, b)
                for m in range(M2 if b < LAST else 1):
                    nc.vector.tensor_scalar(h2[:, m, :], h2_tile(b, m), b2_sb[:, m:m + 1], 0.0,
                                            ALU.add, ALU.max).then_inc(h2_dve, 1)

            def keep_y(b):
                dve.wait_ge(l3_done, b + 1)
                nc.vector.tensor_copy(y_sb[0:1, b * BLOCK:(b + 1) * BLOCK], h2y_ps[0:1, M2, :]
                                      ).then_inc(y_copied, 1)

            def take_own(k, half):
                dve.wait_ge(products_done, 2 * k + half + 1)
                for s in (2, 3):
                    own_block(nc.vector.tensor_copy, k, half, s).then_inc(own_dve, 1)

            def pack(n, k, c):
                halves = 2 * k + (1 if c.stop < QUADS else 2)
                dve.wait_ge(own_act, 2 * halves)
                dve.wait_ge(own_dve, 2 * halves)
                if k >= 2:
                    dve.wait_ge(spread_act, len(SPREAD_ACT) * (k - 1))
                    dve.wait_ge(spread_dve, len(SPREAD_DVE) * (k - 1))
                nc.vector.stream_shuffle(packed[:, k % 2, c], own[:, k % 2, c, HALF:F], SHIFT
                                         ).then_inc(shifted, 1)
                dve.wait_ge(shifted, n + 1)
                nc.vector.copy_predicated(
                    packed[:, k % 2, c],
                    mask_low[:].unsqueeze(1).broadcast_to([P, c.stop - c.start, HALF]),
                    own[:, k % 2, c, 0:HALF]).then_inc(packed_ready, 1)

            def spread_some(n, k, c):
                dve.wait_ge(packed_ready, n + 1)
                if k % 2 == 0 and k // 2 >= 2:
                    dve.wait_ge(l1_done, M1 * (k // 2 - 1))
                for s, q in SPREAD_DVE:
                    spread(nc.vector.tensor_copy, k, c, q, s).then_inc(spread_dve, 1)

            def add_dense(n, k):
                dve.wait_ge(spread_act, len(SPREAD_ACT) * (n + 1))
                dve.wait_ge(spread_dve, len(SPREAD_DVE) * (n + 1))
                half = slice((k % 2) * BATCH, (k % 2 + 1) * BATCH)
                nc.vector.copy_predicated(
                    z[:, (k // 2) % 2, :, half],
                    mask_dense[:].unsqueeze(2).broadcast_to([P, KT, BATCH]),
                    dense_at[:, :, k * BATCH:(k + 1) * BATCH]).then_inc(z_ready, 1)

            place_small(N_SMALL - 1)
            dve.wait_ge(consts_loaded, 48)
            dve.wait_ge(dense_loaded, 16 * HALF)
            dve.wait_ge(weights_loaded, 16 * 5)
            for k in range(N_EVEN):
                b = k // 2 - 1
                place(groups(k + 1)[0])
                if k >= 1:
                    add_dense(k - 1, k - 1)
                if k % 2 == 0 and b >= 1:
                    keep_y(b - 1)
                take_own(k, 0)
                place(groups(k + 1)[2])
                take_own(k, 1)
                pack(k, k, WHOLE)
                if b >= 0 and k % 2 == 1:
                    relu2(b)
                spread_some(k, k, WHOLE)
            k5, k6, k7 = range(N_EVEN, N_BATCH)
            add_dense(k5 - 1, k5 - 1)
            place(groups(k6)[0])
            take_own(k5, 0)
            take_own(k5, 1)
            place(groups(k6)[2])
            pack(k5, k5, WHOLE)
            relu2(LAST - 2)
            spread_some(k5, k5, WHOLE)
            add_dense(k5, k5)
            keep_y(LAST - 2)
            take_own(k6, 0)
            take_own(k6, 1)
            place(groups(k7)[0])
            pack(k6, k6, WHOLE)
            spread_some(k6, k6, WHOLE)
            add_dense(k6, k6)
            place(groups(k7)[2])
            take_own(k7, 0)
            pack(k7, k7, HALVES[0])
            spread_some(k7, k7, HALVES[0])
            take_own(k7, 1)
            pack(k7 + 1, k7, HALVES[1])
            spread_some(k7 + 1, k7, HALVES[1])
            add_dense(k7 + 1, k7)
            relu2(LAST - 1)
            keep_y(LAST - 1)
            relu2(LAST)
            keep_y(LAST)


def layout_constants(rows):
    gather_feats = [f for f in range(F) if f not in small_features(rows)]
    order = gather_feats + small_features(rows)
    first_row = np.concatenate([[0], np.cumsum(rows)[:-1]]).astype(np.int32)
    base = np.tile(first_row[gather_feats], S).reshape(N_GROUPS * CHUNKS, P).T
    pair = {}
    n = 0
    for i in range(F):
        for j in range(i + 1, F):
            pair[i, j] = n
            n += 1
    w1_rows = np.zeros((P, KT), np.int64)
    low_mask = np.zeros((P, HALF), np.int32)
    dense_mask = np.zeros((P, KT), np.int32)
    for a in range(HALF):
        q, k = a // KT, a % KT
        for r in range(F):
            if r == a:
                w1_rows[32 * q + r, k] = n + a
                dense_mask[32 * q + r, k] = 1
                continue
            lo, hi = (HALF + a, HALF + r) if r < a else (a, r)
            f, g = sorted((order[lo], order[hi]))
            w1_rows[32 * q + r, k] = pair[f, g]
            if r > a:
                low_mask[r::32, a] = 1
    return gather_feats, base, w1_rows, low_mask, dense_mask


def kernel(**inputs):
    import concourse.bacc as _bacc
    from concourse.bass_utils import run_bass_kernel_spmd as _run

    x = {k: np.asarray(v) for k, v in inputs.items()}
    tables = [x[f"tbl_{f}"] for f in range(F)]
    rows = [t.shape[0] for t in tables]
    small = small_features(rows)
    gather_feats, base, w1_rows, low_mask, dense_mask = layout_constants(rows)
    ids = x["ids"]

    def sample_order(a):
        return a.reshape(*a.shape[:-1], N_BATCH, QUADS, 4).swapaxes(-1, -2).reshape(a.shape)

    def tiles(w):
        return w.reshape(w.shape[0] // P, P, -1).transpose(1, 0, 2)

    arrays = {
        "table": np.concatenate(tables, axis=0),
        "gather_ids": np.stack([ids[:, gather_feats].reshape(N_GROUPS * CHUNKS, P).T, base], 1),
        "small_ids": ids[:, small].T,
        "low_mask": low_mask,
        "dense_mask": dense_mask,
        "dense": sample_order(x["dense_ctx"].T),
        "identity": np.eye(P, dtype=np.float32).astype(mybir.dt.np(BF16)),
        "w1": x["W_top1"][w1_rows],
        "b1": x["b_top1"].reshape(-1, P).T,
        "w2": tiles(x["W_top2"]),
        "b2": x["b_top2"].reshape(-1, P).T,
        "w3": x["W_top3"].reshape(-1, P).T,
    }
    nc = _bacc.Bacc("TRN2", target_bir_lowering=False, num_devices=1)
    args = []
    for name, a in arrays.items():
        a = arrays[name] = np.ascontiguousarray(a)
        args.append(nc.dram_tensor(name, a.shape, mybir.dt.from_np(a.dtype),
                                   kind="ExternalInput").ap())
    out = nc.dram_tensor("out", (1, S), F32, kind="ExternalOutput").ap()
    build(nc, rows, *args, out)
    y = _run(nc, [arrays], core_ids=[0]).results[0]["out"]
    return y.reshape(N_BATCH, 4, QUADS).swapaxes(1, 2).reshape(S, 1)
```
